# Optimizing a Trainium2 kernel written in Bass

```python
import numpy as np
import jax
import jax.numpy as jnp

def _softmax(x, axis=-1):
    return jax.nn.softmax(x, axis=axis)

def _gelu(x):
    return jax.nn.gelu(x, approximate=True)

def _silu(x):
    return jax.nn.silu(x)

def _sigmoid(x):
    return jax.nn.sigmoid(x)

def _layernorm(x, axis=-1, eps=1e-05):
    m = jnp.mean(x, axis=axis, keepdims=True)
    v = jnp.var(x, axis=axis, keepdims=True)
    return (x - m) / jnp.sqrt(v + eps)

def _scatter_add(tgt, idx, src, axis=0):
    return tgt.at[idx].add(src)

def _segment_sum(src, seg, n):
    return jax.ops.segment_sum(src, seg, n)
kernel_name = 'mk_seq_postln_d1_jaxref_r4_1a34f2'

def setup_inputs(seed: int=0):
    np.random.seed(seed)
    _w = jnp.asarray

    def _L0_attn_setup():
        import jax, jax.numpy as jnp
        import numpy as np
        B, S, D, H = (2, 512, 256, 16)
        DK = D // H
        THETA = 10000.0

        def _rope_tables(seq_len, d_k, theta):
            pos = jnp.arange(seq_len, dtype=jnp.float32)
            dim = jnp.arange(0, d_k, 2, dtype=jnp.float32)
            inv_freq = 1.0 / theta ** (dim / d_k)
            angle = pos[:, None] * inv_freq[None, :]
            angle = jnp.repeat(angle, 2, axis=-1)
            return (jnp.cos(angle), jnp.sin(angle))

        def _apply_rope(x, cos, sin):
            x1 = x[..., ::2]
            x2 = x[..., 1::2]
            x_perm = jnp.stack([-x2, x1], axis=-1).reshape(x.shape)
            return x * cos + x_perm * sin
        key = jax.random.key(seed)
        ks = jax.random.split(key, 5)
        std = np.sqrt(2.0 / (D + D)).astype(np.float32)
        return {'x': jax.random.normal(ks[0], (B, S, D), dtype=jnp.float32), 'Wq': jax.random.normal(ks[1], (D, D), dtype=jnp.float32) * std, 'Wk': jax.random.normal(ks[2], (D, D), dtype=jnp.float32) * std, 'Wv': jax.random.normal(ks[3], (D, D), dtype=jnp.float32) * std, 'Wo': jax.random.normal(ks[4], (D, D), dtype=jnp.float32) * std}
    _L0_attn_in = _L0_attn_setup()

    def _L0_ffn_setup():
        import jax, jax.numpy as jnp
        import numpy as np
        H = 256
        I = 512
        E = 8
        B, S = (2, 1024)
        EPS = 1e-05
        INIT = 0.02

        def _layernorm(x, w, b):
            mu = jnp.mean(x, axis=-1, keepdims=True)
            var = jnp.mean(jnp.square(x - mu), axis=-1, keepdims=True)
            return (x - mu) * jax.lax.rsqrt(var + EPS) * w + b
        key = jax.random.key(seed)
        ks = jax.random.split(key, 9)
        return {'hidden_states': jax.random.normal(ks[0], (B, S, H), jnp.float32), 'ln_w': jnp.ones((H,), jnp.float32), 'ln_b': jnp.zeros((H,), jnp.float32), 'router_w': jax.random.normal(ks[1], (H, E), jnp.float32) * INIT, 'gate_w': jax.random.normal(ks[2], (E, H, I), jnp.float32) * INIT, 'up_w': jax.random.normal(ks[3], (E, H, I), jnp.float32) * INIT, 'down_w': jax.random.normal(ks[4], (E, I, H), jnp.float32) * INIT, 'sh_gate': jax.random.normal(ks[5], (H, I), jnp.float32) * INIT, 'sh_up': jax.random.normal(ks[6], (H, I), jnp.float32) * INIT, 'sh_down': jax.random.normal(ks[7], (I, H), jnp.float32) * INIT}
    _L0_ffn_in = _L0_ffn_setup()
    _d = {'L0_attn_x': _L0_attn_in['x'], 'L0_attn_Wq': _L0_attn_in['Wq'], 'L0_attn_Wk': _L0_attn_in['Wk'], 'L0_attn_Wv': _L0_attn_in['Wv'], 'L0_attn_Wo': _L0_attn_in['Wo'], 'L0_ffn_ln_w': _L0_ffn_in['ln_w'], 'L0_ffn_ln_b': _L0_ffn_in['ln_b'], 'L0_ffn_router_w': _L0_ffn_in['router_w'], 'L0_ffn_gate_w': _L0_ffn_in['gate_w'], 'L0_ffn_up_w': _L0_ffn_in['up_w'], 'L0_ffn_down_w': _L0_ffn_in['down_w'], 'L0_ffn_sh_gate': _L0_ffn_in['sh_gate'], 'L0_ffn_sh_up': _L0_ffn_in['sh_up'], 'L0_ffn_sh_down': _L0_ffn_in['sh_down']}
    _x0 = _d['L0_attn_x']
    _d['L0_attn_x'] = jax.random.normal(jax.random.fold_in(jax.random.key(seed), 1), (4, 1024, 256), dtype=_x0.dtype)
    del _x0
    return _d

def reference(L0_attn_x, L0_attn_Wq, L0_attn_Wk, L0_attn_Wv, L0_attn_Wo, L0_ffn_ln_w, L0_ffn_ln_b, L0_ffn_router_w, L0_ffn_gate_w, L0_ffn_up_w, L0_ffn_down_w, L0_ffn_sh_gate, L0_ffn_sh_up, L0_ffn_sh_down):

    def _L0_attn_ref(x, Wq, Wk, Wv, Wo):
        import jax, jax.numpy as jnp
        import numpy as np
        B, S, D, H = (2, 512, 256, 16)
        DK = D // H
        THETA = 10000.0

        def _rope_tables(seq_len, d_k, theta):
            pos = jnp.arange(seq_len, dtype=jnp.float32)
            dim = jnp.arange(0, d_k, 2, dtype=jnp.float32)
            inv_freq = 1.0 / theta ** (dim / d_k)
            angle = pos[:, None] * inv_freq[None, :]
            angle = jnp.repeat(angle, 2, axis=-1)
            return (jnp.cos(angle), jnp.sin(angle))

        def _apply_rope(x, cos, sin):
            x1 = x[..., ::2]
            x2 = x[..., 1::2]
            x_perm = jnp.stack([-x2, x1], axis=-1).reshape(x.shape)
            return x * cos + x_perm * sin
        seq_len = x.shape[-2]

        def split_heads(t):
            return t.reshape(*t.shape[:-1], H, DK).swapaxes(-3, -2)
        Q = split_heads(jnp.einsum('bsd,od->bso', x, Wq))
        K = split_heads(jnp.einsum('bsd,od->bso', x, Wk))
        V = split_heads(jnp.einsum('bsd,od->bso', x, Wv))
        cos, sin = _rope_tables(seq_len, DK, THETA)
        Q = _apply_rope(Q, cos, sin)
        K = _apply_rope(K, cos, sin)
        scale = 1.0 / np.sqrt(DK).astype(np.float32)
        logits = jnp.einsum('bhnd,bhmd->bhnm', Q, K) * scale
        causal = jnp.tril(jnp.ones((seq_len, seq_len), dtype=bool))
        logits = jnp.where(causal, logits, -jnp.inf)
        probs = jax.nn.softmax(logits, axis=-1)
        attn = jnp.einsum('bhnm,bhmd->bhnd', probs, V)
        attn = attn.swapaxes(-3, -2).reshape(*x.shape[:-1], D)
        return jnp.einsum('bsd,od->bso', attn, Wo)

    def _L0_ffn_ref(hidden_states, ln_w, ln_b, router_w, gate_w, up_w, down_w, sh_gate, sh_up, sh_down):
        import jax, jax.numpy as jnp
        import numpy as np
        H = 256
        I = 512
        E = 8
        B, S = (2, 1024)
        EPS = 1e-05
        INIT = 0.02

        def _layernorm(x, w, b):
            mu = jnp.mean(x, axis=-1, keepdims=True)
            var = jnp.mean(jnp.square(x - mu), axis=-1, keepdims=True)
            return (x - mu) * jax.lax.rsqrt(var + EPS) * w + b
        b, s, h = hidden_states.shape
        normed = _layernorm(hidden_states, ln_w, ln_b)
        xf = normed.reshape(-1, h)
        logits = xf @ router_w
        top_idx = jnp.argmax(logits, axis=-1)
        top_score = jax.nn.sigmoid(jnp.max(logits, axis=-1))

        def body(acc, ew):
            g, u, d, e = ew
            w = jnp.where(top_idx == e, top_score, 0.0)[:, None]
            xe = xf * w
            hmid = jax.nn.silu(xe @ g) * (xe @ u)
            return (acc + hmid @ d, None)
        routed, _ = jax.lax.scan(body, jnp.zeros_like(xf), (gate_w, up_w, down_w, jnp.arange(E)))
        shared = jax.nn.silu(xf @ sh_gate) * (xf @ sh_up) @ sh_down
        moe_out = (routed + shared).reshape(b, s, h)
        return hidden_states + moe_out
    x = L0_attn_x
    x = _layernorm(x + _L0_attn_ref(x, L0_attn_Wq, L0_attn_Wk, L0_attn_Wv, L0_attn_Wo), axis=-1)
    x = _layernorm(x + _L0_ffn_ref(x, L0_ffn_ln_w, L0_ffn_ln_b, L0_ffn_router_w, L0_ffn_gate_w, L0_ffn_up_w, L0_ffn_down_w, L0_ffn_sh_gate, L0_ffn_sh_up, L0_ffn_sh_down), axis=-1)
    return x

_drawn_inputs = setup_inputs


def setup_inputs(seed=0):
    import zlib

    import numpy as np

    out = dict(_drawn_inputs(seed))
    spreads = {'L0_ffn_ln_w': (1.0, 0.6), 'L0_ffn_ln_b': (0.0, 0.8)}
    factors = {'L0_ffn_router_w': 8.0,
     'L0_ffn_gate_w': 8.0,
     'L0_ffn_up_w': 8.0,
     'L0_ffn_down_w': 8.0,
     'L0_ffn_sh_gate': 4.632,
     'L0_ffn_sh_up': 4.541,
     'L0_ffn_sh_down': 4.569}
    for name, (base, spread) in spreads.items():
        noise = np.random.default_rng([zlib.crc32(name.encode()), seed]).standard_normal(out[name].shape)
        drawn = base * np.exp(spread * noise) if base else spread * noise
        out[name] = jnp.asarray(drawn.astype(out[name].dtype))
    for name, factor in factors.items():
        out[name] = (out[name] * factor).astype(out[name].dtype)
    return out
```

```python
from contextlib import ExitStack

import concourse.bass as bass
from concourse import mybir
import numpy as np

F32 = mybir.dt.float32
BF16 = mybir.dt.bfloat16
I32 = mybir.dt.int32
ALU = mybir.AluOpType
ACT = mybir.ActivationFunctionType
X = mybir.AxisListType.X

P = 128
BATCH, SEQ, D = 4, 1024, 256
HEADS = 16
DK = D // HEADS
TOKENS = BATCH * SEQ
DC = D // P
BLOCK = 512
BT = BLOCK // P
BLOCKS = TOKENS // BLOCK
TILES = TOKENS // P
SEQ_TILES = SEQ // P
GROUP = 4
GROUPS = HEADS // GROUP
UNITS = BATCH * GROUPS
GD = GROUP * DK
THETA = 10000.0
EPS = 1e-5
NEG = -3.0e38

PARTS = 3
K_PART = [0, 0, 1, 1, 0, 2]
Q_PART = [0, 1, 0, 1, 2, 0]
ROWS = DK * len(K_PART)
ROWS_MAX = ROWS + PARTS

EXPERTS = 8
INNER = 512
IC = INNER // P
REGION = TOKENS + P
SLOTS = TILES + EXPERTS


def wait(eng, semaphore, value):
    if not isinstance(value, int) or value > 0:
        eng.wait_ge(semaphore, value)


def stand(eng, marker):
    eng.sem_inc(marker, 1)


class Bufs:

    def __init__(self, nc, ctx):
        self.nc, self.ctx = nc, ctx

    def sb(self, name, shape, dtype=F32):
        return self.ctx.enter_context(self.nc.sbuf_tensor(name, shape, dtype))

    def ps(self, name, shape, dtype=F32):
        return self.ctx.enter_context(self.nc.psum_tensor(name, shape, dtype))

    def sem(self, name):
        return self.ctx.enter_context(self.nc.semaphore(name))


def project(nc, io, keep, scratch):
    ident = keep["ident"]
    v_all = keep["v_all"]
    ROPE_TILES = 2 * DC
    with ExitStack() as ctx:
        b = Bufs(nc, ctx)
        w_raw = b.sb("w_raw", [P, 4, DC, D])
        w_t = b.sb("w_t", [P, 3, DC, D])
        cos = b.sb("cos_sb", [P, SEQ])
        sin = b.sb("sin_sb", [P, SEQ])
        x_in = b.sb("x_in", [P, 2, BT, D])
        x_t = b.sb("x_t", [P, 2, DC, BLOCK])
        raw = b.sb("raw", [P, 2, BLOCK])
        swapped = b.sb("swapped", [P, 2, BLOCK])
        cosed = b.sb("cosed", [P, 2, BLOCK])
        rot = b.sb("rot", [P, 2, BLOCK])
        rest = b.sb("rest", [P, 2, BLOCK])
        parts = b.sb("parts", [P, ROPE_TILES, PARTS, BLOCK], BF16)
        turn_ps = b.ps("turn_ps", [P, DC, BLOCK])
        qk_ps = b.ps("qk_ps", [P, ROPE_TILES, BLOCK])
        v_ps = b.ps("v_ps", [P, BT, D])

        w_in = b.sem("w_in")
        tables_in = b.sem("tables_in")
        x_loaded = [b.sem("x_loaded0"), b.sem("x_loaded1")]
        ident_half, ident_made = b.sem("ident_half"), b.sem("ident_made")
        w_turned, w_kept = b.sem("w_turned"), b.sem("w_kept")
        x_turned = b.sem("x_turned")
        xt_first, xt_second = b.sem("xt_first"), b.sem("xt_second")
        qk_done, v_done = b.sem("qk_done"), b.sem("v_done")
        v_kept = b.sem("v_kept")
        raw_ready, cos_ready = b.sem("raw_ready"), b.sem("cos_ready")
        swap_ready, sin_ready, rot_ready = b.sem("swap_ready"), b.sem("sin_ready"), b.sem("rot_ready")
        high_ready, rest_ready, mid_ready, low_ready = (
            b.sem("high_ready"), b.sem("rest_ready"), b.sem("mid_ready"), b.sem("low_ready"))
        stored = [b.sem(f"stored{q}") for q in range(ROPE_TILES)]
        dve_stood = b.sem("dve_stood")

        x_blocks = io["x"].rearrange("(n t p) d -> n p t d", t=BT, p=P)
        block = ctx.enter_context(nc.Block())

        @block.sync
        def _(sp):
            for n, name in enumerate(["Wq", "Wk", "Wv", "Wo"]):
                sp.dma_start(w_raw[:, n], io[name].rearrange("(c p) d -> p c d", p=P)).then_inc(w_in, 16)
            sp.dma_start(cos[:], io["cos"]).then_inc(tables_in, 16)
            sp.dma_start(sin[:], io["sin"]).then_inc(tables_in, 16)

            def load_x(i, odd):
                wait(sp, x_turned, i - 1)
                sp.dma_start(x_in[:, odd], x_blocks[i]).then_inc(x_loaded[odd], 16)

            def store(i, odd, batch):
                for q in range(ROPE_TILES):
                    wait(sp, low_ready, ROPE_TILES * i + q + 1)
                    which, chunk = q // DC, q % DC
                    for g in range(P // GD):
                        unit = batch * GROUPS + chunk * (P // GD) + g
                        dst = scratch["qk"][which][unit]
                        sp.dma_start(dst[:, :, bass.ds(odd * BLOCK, BLOCK)].rearrange("s r t -> r s t"),
                                     parts[g * GD:(g + 1) * GD, q]).then_inc(stored[q], 16)

            load_x(0, 0)

            def step(batch):
                load_x(2 * batch + 1, 1)
                store(2 * batch, 0, batch)
                if not (isinstance(batch, int) and batch == BATCH - 1):
                    load_x(2 * batch + 2, 0)
                store(2 * batch + 1, 1, batch)

            step(0)
            with sp.Fori(1, BATCH - 1) as batch:
                step(batch)
            step(BATCH - 1)
            for q in range(ROPE_TILES):
                sp.wait_ge(stored[q], 32 * BLOCKS)

        @block.tensor
        def _(pe):
            pe.wait_ge(ident_made, 1)
            pe.wait_ge(w_in, 64)
            for n in range(4):
                if n >= 2:
                    pe.wait_ge(w_kept, n - 1)
                bank = turn_ps[:, n % 2].rearrange("p (c o) -> p c o", c=DC)
                for c in range(DC):
                    for o in range(DC):
                        last = nc.tensor.transpose(bank[:, c, o * P:(o + 1) * P],
                                                   w_raw[:, n, o, c * P:(c + 1) * P], ident[:])
                last.then_inc(w_turned, 1)

            def turn_x(i, odd, batch):
                pe.wait_ge(x_loaded[odd], 16 * (batch + 1))
                wait(pe, xt_first, i)
                wait(pe, xt_second, i)
                for c in range(DC):
                    for t in range(BT):
                        last = nc.tensor.transpose(turn_ps[:, c, t * P:(t + 1) * P],
                                                   x_in[:, odd, t, c * P:(c + 1) * P], ident[:])
                last.then_inc(x_turned, 1)

            def project_qk(i, odd):
                pe.wait_ge(xt_first, i + 1)
                pe.wait_ge(xt_second, i + 1)
                for q in range(ROPE_TILES):
                    which, o = q // DC, q % DC
                    wait(pe, raw_ready, ROPE_TILES * (i - 1) + q + 1)
                    for c in range(DC):
                        last = nc.tensor.matmul(qk_ps[:, q], w_t[:, which, c, o * P:(o + 1) * P],
                                                x_t[:, odd, c], start=(c == 0), stop=(c == DC - 1))
                    last.then_inc(qk_done, 1)

            def project_v(i, odd):
                wait(pe, v_kept, i)
                for t in range(BT):
                    for c in range(DC):
                        last = nc.tensor.matmul(v_ps[:, t], x_t[:, odd, c, t * P:(t + 1) * P],
                                                w_t[:, 2, c], start=(c == 0), stop=(c == DC - 1))
                last.then_inc(v_done, 1)

            pe.wait_ge(w_kept, 4)
            turn_x(0, 0, 0)

            def step(batch):
                project_qk(2 * batch, 0)
                turn_x(2 * batch + 1, 1, batch)
                project_v(2 * batch, 0)
                project_qk(2 * batch + 1, 1)
                if not (isinstance(batch, int) and batch == BATCH - 1):
                    turn_x(2 * batch + 2, 0, batch + 1)
                project_v(2 * batch + 1, 1)

            step(0)
            with pe.Fori(1, BATCH - 1) as batch:
                step(batch)
            step(BATCH - 1)

        @block.scalar
        def _(act):
            def copy_weight(n):
                act.wait_ge(w_turned, n + 1)
                dst = w_t[:, n] if n < 3 else keep["wo_t"][:]
                nc.scalar.activation(dst, turn_ps[:, n % 2].rearrange("p (c o) -> p c o", c=DC), ACT.Copy,
                                     scale=DK ** -0.5 if n == 0 else 1.0).then_inc(w_kept, 1)

            for n in range(4):
                copy_weight(n)

            def copy_xt(i, odd):
                act.wait_ge(x_turned, i + 1)
                wait(act, v_done, i - 1)
                nc.scalar.copy(x_t[:, odd, 0], turn_ps[:, 0]).then_inc(xt_first, 1)

            def rope(i, odd, batch):
                for s in range(ROPE_TILES + 2):
                    if s < ROPE_TILES:
                        k = ROPE_TILES * i + s
                        act.wait_ge(qk_done, k + 1)
                        wait(act, rot_ready, k - 1)
                        nc.scalar.copy(raw[:, s % 2], qk_ps[:, s]).then_inc(raw_ready, 1)
                    if 1 <= s <= ROPE_TILES:
                        q = s - 1
                        act.wait_ge(rot_ready, ROPE_TILES * i + q + 1)
                        wait(act, stored[q], 32 * i)
                        nc.scalar.copy(parts[:, q, 0], rot[:, q % 2]).then_inc(high_ready, 1)
                    if s >= 2:
                        q = s - 2
                        act.wait_ge(rest_ready, ROPE_TILES * i + q + 1)
                        nc.scalar.copy(parts[:, q, 1], rest[:, q % 2]).then_inc(mid_ready, 1)

            def keep_v(i, odd, batch):
                act.wait_ge(v_done, i + 1)
                dst = v_all[:, bass.ds(batch * GROUPS, GROUPS), odd * BT:(odd + 1) * BT]
                nc.scalar.copy(dst.rearrange("p g t e -> p t g e"),
                               v_ps[:].rearrange("p t (g e) -> p t g e", g=GROUPS)).then_inc(v_kept, 1)

            copy_xt(0, 0)

            def step(batch):
                rope(2 * batch, 0, batch)
                copy_xt(2 * batch + 1, 1)
                keep_v(2 * batch, 0, batch)
                rope(2 * batch + 1, 1, batch)
                if not (isinstance(batch, int) and batch == BATCH - 1):
                    copy_xt(2 * batch + 2, 0)
                keep_v(2 * batch + 1, 1, batch)

            step(0)
            with act.Fori(1, BATCH - 1) as batch:
                step(batch)
            step(BATCH - 1)

        @block.vector
        def _(dve):
            swap = [r ^ 1 for r in range(32)]

            def copy_xt(i, odd):
                dve.wait_ge(x_turned, i + 1)
                wait(dve, v_done, i - 1)
                nc.vector.tensor_copy(x_t[:, odd, 1], turn_ps[:, 1]).then_inc(xt_second, 1)

            def rope(i, odd):
                for s in range(ROPE_TILES + 2):
                    if s < ROPE_TILES:
                        k = ROPE_TILES * i + s
                        dve.wait_ge(raw_ready, k + 1)
                        wait(dve, rot_ready, k - 1)
                        stand(dve, dve_stood)
                        nc.vector.stream_shuffle(swapped[:, s % 2], raw[:, s % 2], swap).then_inc(swap_ready, 1)
                        dve.wait_ge(swap_ready, k + 1)
                        nc.vector.tensor_tensor(swapped[:, s % 2], swapped[:, s % 2],
                                                sin[:, odd * BLOCK:(odd + 1) * BLOCK],
                                                ALU.mult).then_inc(sin_ready, 1)
                    if s >= 2:
                        q = s - 2
                        dve.wait_ge(mid_ready, ROPE_TILES * i + q + 1)
                        nc.vector.tensor_tensor(parts[:, q, 2], rest[:, q % 2], parts[:, q, 1],
                                                ALU.subtract).then_inc(low_ready, 1)
                    if s < ROPE_TILES:
                        dve.wait_ge(cos_ready, k + 1)
                        dve.wait_ge(sin_ready, k + 1)
                        wait(dve, rest_ready, k - 1)
                        nc.vector.tensor_tensor(rot[:, s % 2], cosed[:, s % 2], swapped[:, s % 2],
                                                ALU.add).then_inc(rot_ready, 1)

            dve.wait_ge(tables_in, 32)
            copy_xt(0, 0)

            def step(batch):
                rope(2 * batch, 0)
                copy_xt(2 * batch + 1, 1)
                rope(2 * batch + 1, 1)
                if not (isinstance(batch, int) and batch == BATCH - 1):
                    copy_xt(2 * batch + 2, 0)

            step(0)
            with dve.Fori(1, BATCH - 1) as batch:
                step(batch)
            step(BATCH - 1)

        @block.gpsimd
        def _(pool):
            nc.gpsimd.memset(ident[:], 0.0).then_inc(ident_half, 1)
            pool.wait_ge(ident_half, 1)
            nc.gpsimd.affine_select(out=ident[:], in_=ident[:], compare_op=ALU.not_equal, fill=1.0, base=0,
                                    pattern=[[-1, P]], channel_multiplier=1).then_inc(ident_made, 1)
            pool.wait_ge(tables_in, 32)

            def step(batch):
                for odd in range(2):
                    i = 2 * batch + odd
                    for s in range(ROPE_TILES + 1):
                        if s < ROPE_TILES:
                            k = ROPE_TILES * i + s
                            pool.wait_ge(raw_ready, k + 1)
                            wait(pool, rot_ready, k - 1)
                            nc.gpsimd.tensor_tensor(cosed[:, s % 2], raw[:, s % 2],
                                                    cos[:, odd * BLOCK:(odd + 1) * BLOCK],
                                                    ALU.mult).then_inc(cos_ready, 1)
                        if s >= 1:
                            q = s - 1
                            k = ROPE_TILES * i + q
                            pool.wait_ge(high_ready, k + 1)
                            wait(pool, low_ready, k - 1)
                            nc.gpsimd.tensor_tensor(rest[:, q % 2], rot[:, q % 2], parts[:, q, 0],
                                                    ALU.subtract).then_inc(rest_ready, 1)

            step(0)
            with pool.Fori(1, BATCH - 1) as batch:
                step(batch)
            step(BATCH - 1)


def rope_tables():
    dim = np.arange(0, DK, 2, dtype=np.float32)
    inv_freq = (np.float32(1.0) / np.power(np.float32(THETA), dim / np.float32(DK))).astype(np.float32)
    angle = np.arange(SEQ, dtype=np.float32)[None, :] * np.repeat(inv_freq, 2)[:, None]
    sign = np.where(np.arange(DK) % 2 == 0, -1.0, 1.0).astype(np.float32)[:, None]
    return np.tile(np.cos(angle), (P // DK, 1)), np.tile(np.sin(angle) * sign, (P // DK, 1))


class Unit:

    RING = 3

    def __init__(self, i, slot, turn):
        self.i, self.slot, self.turn = i, slot, turn

    def ahead(self, k):
        return Unit(self.i + k, (self.slot + k) % self.RING, self.turn + (self.slot + k) // self.RING)

    def exists(self):
        return not isinstance(self.i, int) or self.i < UNITS

    @staticmethod
    def number(i):
        return Unit(i, i % Unit.RING, i // Unit.RING)


def each_unit(eng, step):
    for i in range(2):
        step(Unit.number(i))
    with eng.Fori(0, (UNITS - 4) // Unit.RING) as turn:
        for k in range(2, 2 + Unit.RING):
            step(Unit(turn * Unit.RING + k, k % Unit.RING, turn + k // Unit.RING))
    for i in range(UNITS - 2, UNITS):
        step(Unit.number(i))


def attend_plan():
    order = [[0, 3, 2, 1], [0, 4, 5, 6, 7, 1, 2, 3]]
    steps = [(c, mt, max(mt - BT * c, 0) * P) for c in range(2) for mt in order[c]]
    pieces = []
    for t in range(SEQ_TILES):
        for chunk in range(t // BT + 1):
            keys = min((t + 1) * P - chunk * BLOCK, BLOCK)
            heads = {P: 4, 2 * P: 2}.get(keys, 1)
            pieces += [(h, heads, t, chunk, keys) for h in range(0, GROUP, heads)]
    rest, early = [4, 1, 2, 3, 4, 4, 3, 3], [2, 4, 4, 4]
    assert sum(rest) + sum(early) == len(pieces) and len(rest + early) == len(steps)
    return steps, pieces, rest, early


def attend(nc, io, keep, scratch):
    ident, v_all = keep["ident"], keep["v_all"]
    RING = Unit.RING
    steps, pieces, rest, early = attend_plan()
    STEPS, PIECES, EARLY = len(steps), len(pieces), sum(early)
    DIAGONAL = [s for s, (c, mt, _) in enumerate(steps) if mt >= BT * c]
    STACK_DMAS = 2 * len(K_PART)
    PER_TURN = EXPERTS // ((UNITS - 4) // RING)
    with ExitStack() as ctx:
        b = Bufs(nc, ctx)
        k_stack = b.sb("k_stack", [P, RING, GROUP, SEQ], BF16)
        q_stack = b.sb("q_stack", [P, RING, GROUP, SEQ], BF16)
        probs = b.sb("probs", [P, RING, GROUP, BLOCK])
        v_ones = b.sb("v_ones", [P, RING, SEQ_TILES, GROUP, 2 * DK])
        maxima = b.sb("maxima", [P, RING, 2, GROUP, SEQ_TILES])
        neg_max = b.sb("neg_max", [GROUP * SEQ_TILES, P])
        neg_rest = b.sb("neg_rest", [GROUP * SEQ_TILES, P])
        neg_parts = b.sb("neg_parts", [GROUP * SEQ_TILES, PARTS, P], BF16)
        out_t = b.sb("out_t", [P, 2, BLOCK])
        recip = b.sb("recip", [P, 2, BT, GROUP])
        heads_out = b.sb("heads_out", [P, 2, BT, GROUP, DK])
        ident_bf = b.sb("ident_bf", [P, P], BF16)
        mask = b.sb("mask", [P, P], BF16)
        scores_ps = b.ps("scores_ps", [P, 2, 2, BLOCK])
        max_ps = b.ps("max_ps", [P, 2, BLOCK])
        out_ps = b.ps("out_ps", [P, BLOCK])
        turn_ps = b.ps("turn_ps2", [P, BT, P])

        loaded = [b.sem(f"stacks_loaded{r}") for r in range(RING)]
        neg_loaded = b.sem("neg_loaded")
        consts_half, consts_made, k_ones = b.sem("consts_half"), b.sem("consts_made"), b.sem("k_ones")
        piece_done, piece_reduced = b.sem("piece_done"), b.sem("piece_reduced")
        combined, max_turned = b.sem("combined"), b.sem("max_turned")
        neg_copied, neg_split = b.sem("neg_copied"), b.sem("neg_split")
        v_grouped = b.sem("v_grouped")
        scores_done, exp_done, masked = b.sem("scores_done"), b.sem("exp_done"), b.sem("masked")
        pv_done, out_copied = b.sem("pv_done"), b.sem("out_copied")
        out_turned, recip_done, normed = b.sem("out_turned"), b.sem("recip_done"), b.sem("normed")
        heads_stored = [b.sem("heads_stored0"), b.sem("heads_stored1")]
        pool_stood = b.sem("pool_stood")
        block = ctx.enter_context(nc.Block())

        @block.sync
        def _(sp):
            def load(u):
                if not u.exists():
                    return
                wait(sp, scores_done, 2 * STEPS * (u.i - 2))
                for stack, part, src in ((k_stack, K_PART, scratch["qk"][1]), (q_stack, Q_PART, scratch["qk"][0])):
                    for e, n in enumerate(part):
                        sp.dma_start(stack[e * DK:(e + 1) * DK, u.slot],
                                     src[u.i, n].rearrange("(h d) t -> d h t", d=DK)).then_inc(loaded[u.slot], 16)

            def send_neg(u):
                if not u.exists():
                    return
                sp.wait_ge(neg_split, 4 * (u.i + 1))
                for n in range(PARTS):
                    dst = q_stack[ROWS + n:ROWS + n + 1, u.slot]
                    sp.dma_start(dst.rearrange("o h (t c) -> o (h t) c", c=P),
                                 neg_parts[:, n]).then_inc(neg_loaded, 16)

            def store_heads(u, c):
                if isinstance(u.i, int) and u.i < 0:
                    return
                sp.wait_ge(normed, 2 * u.i + c + 1)
                sp.dma_start(scratch["heads"][u.i, c],
                             heads_out[:, c].rearrange("p t h d -> p (t h d)")).then_inc(heads_stored[c], 16)

            def step(u):
                load(u.ahead(2))
                store_heads(u.ahead(-1), 1)
                store_heads(u, 0)
                send_neg(u.ahead(1))

            load(Unit.number(0))
            load(Unit.number(1))
            send_neg(Unit.number(0))
            each_unit(sp, step)
            store_heads(Unit.number(UNITS - 1), 1)
            for c in range(2):
                sp.wait_ge(heads_stored[c], 16 * UNITS)

        @block.tensor
        def _(pe):
            def find_max(u, first, count):
                if not u.exists():
                    return
                for n in range(first, first + count):
                    h0, heads, t, chunk, keys = pieces[n]
                    if n == 0:
                        pe.wait_ge(loaded[u.slot], 16 * STACK_DMAS * (u.turn + 1))
                    wait(pe, piece_reduced, PIECES * u.i + n - 1)
                    for k in range(heads):
                        bank = max_ps[:, n % 2, k * keys:(k + 1) * keys]
                        diagonal = chunk == t // BT
                        last = nc.tensor.matmul(bank, q_stack[:ROWS, u.slot, h0 + k, t * P:(t + 1) * P],
                                                k_stack[:ROWS, u.slot, h0 + k, chunk * BLOCK:chunk * BLOCK + keys],
                                                start=True, stop=not diagonal)
                        if diagonal:
                            last = nc.tensor.matmul(bank[:, keys - P:], ident_bf[:], mask[:],
                                                    start=False, stop=True)
                    last.then_inc(piece_done, 1)

            def turn_max(u):
                if not u.exists():
                    return
                pe.wait_ge(combined, u.i + 1)
                wait(pe, normed, 2 * u.i - 1)
                nc.tensor.transpose(turn_ps[:GROUP * SEQ_TILES, 0],
                                    maxima[:, u.slot, 0].rearrange("p h t -> p (h t)"),
                                    ident[:]).then_inc(max_turned, 1)

            def score(u, s):
                c, mt, n0 = steps[s]
                if s == 0:
                    pe.wait_ge(neg_loaded, 16 * PARTS * (u.i + 1))
                for pair in range(2):
                    wait(pe, exp_done, 2 * (STEPS * u.i + s) + pair - 1)
                    for k in range(2):
                        h = 2 * pair + k
                        last = nc.tensor.matmul(scores_ps[:, pair, k, n0:],
                                                k_stack[:ROWS_MAX, u.slot, h, mt * P:(mt + 1) * P],
                                                q_stack[:ROWS_MAX, u.slot, h, c * BLOCK + n0:(c + 1) * BLOCK],
                                                start=True, stop=True)
                    last.then_inc(scores_done, 1)

            def times_v(u, s):
                if isinstance(u.i, int) and u.i < 0:
                    return
                c, mt, n0 = steps[s]
                if s == 0:
                    pe.wait_ge(v_grouped, u.i + 1)
                if mt == 0:
                    wait(pe, out_copied, 2 * u.i + c)
                if s in DIAGONAL:
                    pe.wait_ge(masked, len(DIAGONAL) * u.i + DIAGONAL.index(s) + 1)
                else:
                    pe.wait_ge(exp_done, 2 * (STEPS * u.i + s) + 2)
                last_of_chunk = s + 1 == STEPS or steps[s + 1][0] != c
                for h in range(GROUP):
                    last = nc.tensor.matmul(out_ps[32 * h:32 * h + 32, n0:], v_ones[:, u.slot, mt, h],
                                            probs[:, s % RING, h, n0:], start=(mt == 0), stop=last_of_chunk)
                last.then_inc(pv_done, 1)

            def turn_out(u, c):
                if isinstance(u.i, int) and u.i < 0:
                    return
                pe.wait_ge(out_copied, 2 * u.i + c + 1)
                wait(pe, normed, 2 * u.i + c)
                if c == 1:
                    wait_neg = u.ahead(1)
                    if wait_neg.exists():
                        pe.wait_ge(neg_copied, wait_neg.i + 1)
                for t in range(BT):
                    last = nc.tensor.transpose(turn_ps[:, t], out_t[:, c, t * P:(t + 1) * P], ident[:])
                last.then_inc(out_turned, 1)

            def step(u):
                begun = PIECES - sum(rest)
                for s in range(STEPS):
                    if s == 2:
                        turn_out(u.ahead(-1), 1)
                    if s == 6:
                        turn_out(u, 0)
                    if s == 9:
                        turn_max(u.ahead(1))
                    score(u, s)
                    if s < len(rest):
                        find_max(u.ahead(1), begun, rest[s])
                        begun += rest[s]
                    else:
                        n = s - len(rest)
                        find_max(u.ahead(2), sum(early[:n]), early[n])
                    times_v(u if s else u.ahead(-1), (s - 1) % STEPS)

            pe.wait_ge(consts_made, 3)
            pe.wait_ge(k_ones, 1)
            find_max(Unit.number(0), 0, PIECES)
            find_max(Unit.number(1), 0, EARLY)
            turn_max(Unit.number(0))
            each_unit(pe, step)
            times_v(Unit.number(UNITS - 1), STEPS - 1)
            turn_out(Unit.number(UNITS - 1), 1)

        @block.scalar
        def _(act):
            def exp(u, s):
                c, mt, n0 = steps[s]
                wait(act, pv_done, STEPS * u.i + s - 2)
                for pair in range(2):
                    act.wait_ge(scores_done, 2 * (STEPS * u.i + s) + pair + 1)
                    nc.scalar.activation(probs[:, s % RING, 2 * pair:2 * pair + 2, n0:],
                                         scores_ps[:, pair, :, n0:], ACT.Exp).then_inc(exp_done, 1)

            def copy_out(u, c):
                if isinstance(u.i, int) and u.i < 0:
                    return
                act.wait_ge(pv_done, STEPS * u.i + (BT if c == 0 else STEPS))
                wait(act, out_turned, 2 * u.i + c - 1)
                nc.scalar.copy(out_t[:, c], out_ps[:]).then_inc(out_copied, 1)

            def negate(u):
                if not u.exists():
                    return
                act.wait_ge(max_turned, u.i + 1)
                wait(act, neg_split, 4 * u.i)
                nc.scalar.mul(neg_max[:], turn_ps[:GROUP * SEQ_TILES, 0], -1.0).then_inc(neg_copied, 1)

            def load_weights(u):
                if isinstance(u.i, int) or u.slot == 1:
                    return
                name, turn = ("gate", u.turn) if u.slot == 2 else ("up", u.turn - 1)
                for k in range(PER_TURN):
                    e = PER_TURN * turn + k
                    act.dma_start(keep[name][:, bass.ds(e, 1)], io[f"{name}_w"][bass.ds(e, 1)].rearrange(
                        "e (c p) n -> p e c n", p=P)).then_inc(keep["weights_in"], 16)

            def step(u):
                for s in range(STEPS):
                    if s == 1:
                        copy_out(u.ahead(-1), 1)
                    if s == 5:
                        copy_out(u, 0)
                    if s == 8:
                        load_weights(u)
                    if s == 9:
                        negate(u.ahead(1))
                    exp(u, s)

            negate(Unit.number(0))
            each_unit(act, step)
            copy_out(Unit.number(UNITS - 1), 1)

        @block.vector
        def _(dve):
            def reduce(u, first, count):
                if not u.exists():
                    return
                for n in range(first, first + count):
                    h0, heads, t, chunk, keys = pieces[n]
                    if n == 0:
                        wait(dve, max_turned, u.i - 2)
                    dve.wait_ge(piece_done, PIECES * u.i + n + 1)
                    nc.vector.tensor_reduce(maxima[:, u.slot, chunk, h0:h0 + heads, t],
                                            max_ps[:, n % 2, :heads * keys].rearrange("p (h k) -> p h k", h=heads),
                                            X, ALU.max).then_inc(piece_reduced, 1)

            def combine(u):
                if not u.exists():
                    return
                dve.wait_ge(piece_reduced, PIECES * (u.i + 1))
                both = maxima[:, u.slot, :, :, BT:]
                nc.vector.tensor_tensor(both[:, 0], both[:, 0], both[:, 1], ALU.max).then_inc(combined, 1)

            def normalise(u, c):
                if isinstance(u.i, int) and u.i < 0:
                    return
                k = 2 * u.i + c
                dve.wait_ge(out_turned, k + 1)
                wait(dve, heads_stored[c], 16 * u.i)
                rows = turn_ps[:].rearrange("p t (h e) -> p t h e", h=GROUP)
                nc.vector.reciprocal(recip[:, c], rows[:, :, :, DK]).then_inc(recip_done, 1)
                dve.wait_ge(recip_done, k + 1)
                nc.vector.tensor_tensor(heads_out[:, c], rows[:, :, :, :DK],
                                        recip[:, c].unsqueeze(3).to_broadcast([P, BT, GROUP, DK]),
                                        ALU.mult).then_inc(normed, 1)

            def step(u):
                begun = PIECES - sum(rest)
                for s in range(STEPS):
                    if s == 3:
                        normalise(u.ahead(-1), 1)
                    if s == 7:
                        normalise(u, 0)
                    if s == 8:
                        combine(u.ahead(1))
                    if s < len(rest):
                        reduce(u.ahead(1), begun, rest[s])
                        begun += rest[s]
                    else:
                        n = s - len(rest)
                        reduce(u.ahead(2), sum(early[:n]), early[n])

            nc.vector.memset(k_stack[ROWS:ROWS_MAX], 1.0).then_inc(k_ones, 1)
            reduce(Unit.number(0), 0, PIECES)
            combine(Unit.number(0))
            reduce(Unit.number(1), 0, EARLY)
            each_unit(dve, step)
            normalise(Unit.number(UNITS - 1), 1)

        @block.gpsimd
        def _(pool):
            nc.gpsimd.memset(v_ones[:], 1.0).then_inc(consts_made, 1)
            nc.gpsimd.tensor_copy(ident_bf[:], ident[:]).then_inc(consts_made, 1)
            nc.gpsimd.memset(mask[:], 0.0).then_inc(consts_half, 1)
            pool.wait_ge(consts_half, 1)
            nc.gpsimd.affine_select(out=mask[:], in_=mask[:], compare_op=ALU.is_ge, fill=NEG, base=0,
                                    pattern=[[-1, P]], channel_multiplier=1).then_inc(consts_made, 1)

            def group_v(u):
                if not u.exists():
                    return
                wait(pool, pv_done, STEPS * (u.i - 2))
                stand(pool, pool_stood)
                nc.gpsimd.tensor_copy(v_ones[:, u.slot, :, :, :DK],
                                      v_all[:, u.i].rearrange("p t (h d) -> p t h d", h=GROUP)).then_inc(v_grouped, 1)

            def split_neg(u):
                if not u.exists():
                    return
                n = 4 * u.i
                pool.wait_ge(neg_copied, u.i + 1)
                wait(pool, neg_loaded, 16 * PARTS * u.i)
                stand(pool, pool_stood)
                nc.gpsimd.tensor_copy(neg_parts[:, 0], neg_max[:]).then_inc(neg_split, 1)
                pool.wait_ge(neg_split, n + 1)
                nc.gpsimd.tensor_tensor(neg_rest[:], neg_max[:], neg_parts[:, 0], ALU.subtract).then_inc(neg_split, 1)
                pool.wait_ge(neg_split, n + 2)
                stand(pool, pool_stood)
                nc.gpsimd.tensor_copy(neg_parts[:, 1], neg_rest[:]).then_inc(neg_split, 1)
                pool.wait_ge(neg_split, n + 3)
                nc.gpsimd.tensor_tensor(neg_parts[:, 2], neg_rest[:], neg_parts[:, 1], ALU.subtract).then_inc(neg_split, 1)

            def drop_later_keys(u, s):
                c, mt, n0 = steps[s]
                pool.wait_ge(exp_done, 2 * (STEPS * u.i + s) + 2)
                stand(pool, pool_stood)
                tile = probs[:, s % RING, :, n0:n0 + P]
                nc.gpsimd.affine_select(out=tile, in_=tile, compare_op=ALU.is_ge, fill=0.0, base=0,
                                        pattern=[[0, GROUP], [1, P]], channel_multiplier=-1).then_inc(masked, 1)

            def step(u):
                for s in range(STEPS):
                    if s in DIAGONAL:
                        drop_later_keys(u, s)
                    if s == 8:
                        group_v(u.ahead(1))
                    if s == 9:
                        split_neg(u.ahead(1))

            pool.wait_ge(consts_made, 1)
            group_v(Unit.number(0))
            split_neg(Unit.number(0))
            each_unit(pool, step)


def by_batch(eng, step):
    step(0)
    with eng.Fori(1, BATCH - 1) as batch:
        step(batch)
    step(BATCH - 1)


def mix(nc, io, keep, scratch):
    ident, wo_t, acc = keep["ident"], keep["wo_t"], keep["acc"]
    chosen_all, rank_all, counts = keep["chosen_all"], keep["rank_all"], keep["counts"]
    with ExitStack() as ctx:
        b = Bufs(nc, ctx)
        sh_gate = b.sb("sh_gate_sb", [P, DC, INNER])
        sh_up = b.sb("sh_up_sb", [P, DC, INNER])
        sh_down = b.sb("sh_down_sb", [P, IC, D])
        router = b.sb("router_sb", [P, DC, EXPERTS])
        ln_w = b.sb("ln_w_sb", [P, D])
        ln_b = b.sb("ln_b_sb", [P, D])
        res = b.sb("res", [P, 2, BT, D])
        heads = b.sb("heads_in", [P, 2, BT, GROUPS, GD])
        heads_t = b.sb("heads_t", [P, DC, BLOCK])
        x1 = b.sb("x1", [P, 2, BT, D])
        xf = b.sb("xf", [P, BT, D])
        xf_t = b.sb("xf_t", [P, 2, DC, BLOCK])
        row = b.sb("row", [P, BT, D])
        silu = b.sb("silu", [P, 2, INNER])
        hidden = b.sb("hidden", [P, 2, INNER])
        hidden_t = b.sb("hidden_t", [P, 2, INNER])
        stats = b.sb("stats", [P, BT, 6])
        moments = b.sb("moments", [P, BT, 2])
        var_eps = b.sb("var_eps", [P, BT])
        rstd = b.sb("rstd", [P, BT])
        minus_half = b.sb("minus_half", [P, BT])
        top = b.sb("top", [P, BT])
        score = b.sb("score", [P, 2, BT])
        is_top = b.sb("is_top", [P, BT, EXPERTS])
        candidate = b.sb("candidate", [P, BT, EXPERTS])
        number = b.sb("number", [P, BT, EXPERTS])
        number_i = b.sb("number_i", [P, BT, EXPERTS], I32)
        first = b.sb("first", [P, BT])
        chosen = b.sb("chosen", [P, BT, EXPERTS])
        chosen_bf = b.sb("chosen_bf", [P, BT + 1, EXPERTS], BF16)
        rank = b.sb("rank", [P, BT, EXPERTS])
        place = b.sb("place", [P, BT])
        place_i = b.sb("place_i", [P, 2, BT], I32)
        before = b.sb("before", [P, P], BF16)
        ones = b.sb("ones", [P, P], BF16)
        front_ps = b.ps("front_ps", [P, DC, BLOCK])
        gate_ps = b.ps("gate_ps", [P, 2, INNER])
        up_ps = b.ps("up_ps", [P, 2, INNER])
        hidden_ps = b.ps("hidden_ps", [P, INNER])
        down_ps = b.ps("down_ps", [P, D])

        ffn_in, small_in = b.sem("ffn_in"), b.sem("small_in")
        res_in = [b.sem("res_in0"), b.sem("res_in1")]
        heads_in = [b.sem("heads_in0"), b.sem("heads_in1")]
        const_step, vec_const = b.sem("const_step"), b.sem("vec_const")
        heads_turned, heads_t_kept = b.sem("heads_turned"), b.sem("heads_t_kept")
        wo_done, x1_made, xf_made = b.sem("wo_done"), b.sem("x1_made"), b.sem("xf_made")
        xf_turned, xf_t_kept = b.sem("xf_turned"), b.sem("xf_t_kept")
        routed, chosen_made, ranked, placed = (
            b.sem("routed"), b.sem("chosen_made"), b.sem("ranked"), b.sem("placed"))
        moments_made, rstd_made = b.sem("moments_made"), b.sem("rstd_made")
        pool_step = b.sem("pool_step")
        top_made, tanh_made, score_made, row_made, scattered = (
            b.sem("top_made"), b.sem("tanh_made"), b.sem("score_made"), b.sem("row_made"), b.sem("scattered"))
        front_step = b.sem("front_step")
        gate_done, up_done, silu_made, hidden_made = (
            b.sem("gate_done"), b.sem("up_done"), b.sem("silu_made"), b.sem("hidden_made"))
        hidden_turned, hidden_t_kept, down_done, added = (
            b.sem("hidden_turned"), b.sem("hidden_t_kept"), b.sem("down_done"), b.sem("added"))
        block = ctx.enter_context(nc.Block())
        x_blocks = io["x"].rearrange("(n t p) d -> n p t d", t=BT, p=P)
        dve_stood, pool_stood = b.sem("dve_stood"), b.sem("pool_stood")
        VEC_STEPS = 16

        @block.sync
        def _(sp):
            def load(i, batch, odd):
                wait(sp, xf_made, i - 1)
                wait(sp, heads_turned, i - 1)
                sp.dma_start(res[:, odd], x_blocks[i]).then_inc(res_in[odd], 16)
                for g in range(GROUPS):
                    sp.dma_start(heads[:, odd, :, g], scratch["heads"][batch * GROUPS + g, odd].rearrange(
                        "p (t e) -> p t e", t=BT)).then_inc(heads_in[odd], 16)

            load(0, 0, 0)
            sp.dma_start(sh_gate[:], io["sh_gate"].rearrange("(c p) n -> p c n", p=P)).then_inc(ffn_in, 16)
            sp.dma_start(sh_up[:], io["sh_up"].rearrange("(c p) n -> p c n", p=P)).then_inc(ffn_in, 16)
            sp.dma_start(sh_down[:], io["sh_down"].rearrange("(c p) n -> p c n", p=P)).then_inc(ffn_in, 16)
            for e in range(EXPERTS):
                sp.dma_start(keep["down"][:, e], io["down_w"][e].rearrange("(c p) n -> p c n", p=P)).then_inc(
                    keep["down_in"], 16)

            def step(batch):
                load(2 * batch + 1, batch, 1)
                if not (isinstance(batch, int) and batch == BATCH - 1):
                    load(2 * batch + 2, batch + 1, 0)

            by_batch(sp, step)

        @block.tensor
        def _(pe):
            def turn_heads(i, batch, odd):
                pe.wait_ge(heads_in[odd], 16 * GROUPS * (batch + 1))
                wait(pe, placed, i)
                for c in range(DC):
                    for t in range(BT):
                        last = nc.tensor.transpose(
                            front_ps[:, c, t * P:(t + 1) * P],
                            heads[:, odd, t, 2 * c:2 * c + 2].rearrange("p g e -> p (g e)"), ident[:])
                last.then_inc(heads_turned, 1)

            def times_wo(i, batch, odd):
                pe.wait_ge(heads_t_kept, i + 1)
                for t in range(BT):
                    for c in range(DC):
                        last = nc.tensor.matmul(front_ps[:, t // 2, t % 2 * D:(t % 2 + 1) * D],
                                                heads_t[:, c, t * P:(t + 1) * P], wo_t[:, c],
                                                start=(c == 0), stop=(c == DC - 1))
                last.then_inc(wo_done, 1)

            def turn_xf(i, batch, odd):
                pe.wait_ge(xf_made, i + 1)
                for c in range(DC):
                    for t in range(BT):
                        last = nc.tensor.transpose(front_ps[:, c, t * P:(t + 1) * P],
                                                   xf[:, t, c * P:(c + 1) * P], ident[:])
                last.then_inc(xf_turned, 1)

            def route(i, batch, odd):
                pe.wait_ge(xf_t_kept, i + 1)
                for t in range(BT):
                    for c in range(DC):
                        last = nc.tensor.matmul(front_ps[:, 0, t * EXPERTS:(t + 1) * EXPERTS],
                                                xf_t[:, odd, c, t * P:(t + 1) * P], router[:, c],
                                                start=(c == 0), stop=(c == DC - 1))
                last.then_inc(routed, 1)

            def count_ranks(i, batch, odd):
                pe.wait_ge(chosen_made, i + 1)
                out = front_ps[:, 1, :(BT + 1) * EXPERTS].rearrange("p (t e) -> p t e", e=EXPERTS)
                nc.tensor.matmul(out, before[:], chosen_bf[:], start=True, stop=False)
                for t in range(BT):
                    last = nc.tensor.matmul(out[:, t + 1:], ones[:], chosen_bf[:, t].unsqueeze(1).to_broadcast(
                        [P, BT - t, EXPERTS]), start=False, stop=(t == BT - 1))
                last.then_inc(ranked, 1)

            def gate(i, t, odd):
                pe.wait_ge(xf_t_kept, i + 1)
                wait(pe, silu_made, BT * i + t - 1)
                for c in range(DC):
                    last = nc.tensor.matmul(gate_ps[:, t % 2], xf_t[:, odd, c, t * P:(t + 1) * P], sh_gate[:, c],
                                            start=(c == 0), stop=(c == DC - 1))
                last.then_inc(gate_done, 1)

            def up(i, t, odd):
                wait(pe, hidden_made, BT * i + t - 1)
                for c in range(DC):
                    last = nc.tensor.matmul(up_ps[:, t % 2], xf_t[:, odd, c, t * P:(t + 1) * P], sh_up[:, c],
                                            start=(c == 0), stop=(c == DC - 1))
                last.then_inc(up_done, 1)

            def turn_hidden(i, t):
                pe.wait_ge(hidden_made, BT * i + t + 1)
                wait(pe, hidden_t_kept, BT * i + t)
                for c in range(IC):
                    last = nc.tensor.transpose(hidden_ps[:, c * P:(c + 1) * P],
                                               hidden[:, t % 2, c * P:(c + 1) * P], ident[:])
                last.then_inc(hidden_turned, 1)

            def down(i, t):
                pe.wait_ge(hidden_t_kept, BT * i + t + 1)
                wait(pe, added, BT * i + t)
                for c in range(IC):
                    last = nc.tensor.matmul(down_ps[:], hidden_t[:, t % 2, c * P:(c + 1) * P], sh_down[:, c],
                                            start=(c == 0), stop=(c == IC - 1))
                last.then_inc(down_done, 1)

            def front_alone(n, batch, odd):
                for part in (turn_heads, times_wo, turn_xf, route, count_ranks):
                    part(n, batch, odd)

            def block_step(i, odd, nxt):
                def front(part):
                    if nxt is not None:
                        part(i + 1, nxt, 1 - odd)

                gate(i, 0, odd)
                up(i, 0, odd)
                front(turn_heads)
                gate(i, 1, odd)
                turn_hidden(i, 0)
                up(i, 1, odd)
                front(times_wo)
                down(i, 0)
                gate(i, 2, odd)
                turn_hidden(i, 1)
                up(i, 2, odd)
                down(i, 1)
                gate(i, 3, odd)
                turn_hidden(i, 2)
                up(i, 3, odd)
                front(turn_xf)
                down(i, 2)
                turn_hidden(i, 3)
                front(route)
                down(i, 3)
                front(count_ranks)

            def step(batch):
                block_step(2 * batch, 0, batch)
                last = isinstance(batch, int) and batch == BATCH - 1
                block_step(2 * batch + 1, 1, None if last else batch + 1)

            pe.wait_ge(const_step, 6)
            pe.wait_ge(small_in, 16 * 3)
            front_alone(0, 0, 0)
            pe.wait_ge(ffn_in, 48)
            by_batch(pe, step)

        @block.scalar
        def _(act):
            act.dma_start(router[:], io["router_w"].rearrange("(c p) n -> p c n", p=P)).then_inc(small_in, 16)
            act.dma_start(ln_w[:], io["ln_w"].partition_broadcast(P)).then_inc(small_in, 16)
            act.dma_start(ln_b[:], io["ln_b"].partition_broadcast(P)).then_inc(small_in, 16)

            def keep_heads(i, batch, odd):
                act.wait_ge(heads_turned, i + 1)
                wait(act, wo_done, i)
                nc.scalar.copy(heads_t[:], front_ps[:]).then_inc(heads_t_kept, 1)

            def keep_xf(i, batch, odd):
                act.wait_ge(xf_turned, i + 1)
                wait(act, up_done, BT * (i - 1))
                nc.scalar.copy(xf_t[:, odd], front_ps[:]).then_inc(xf_t_kept, 1)

            def scale_rows(i, batch, odd):
                act.wait_ge(top_made, i + 1)
                nc.scalar.activation(score[:, 0], top[:], ACT.Tanh, scale=0.5).then_inc(tanh_made, 1)
                act.wait_ge(score_made, i + 1)
                wait(act, scattered, 16 * BT * i)
                for t in range(BT):
                    last = nc.scalar.activation(row[:, t], xf[:, t], ACT.Copy, scale=score[:, 1, t:t + 1])
                last.then_inc(row_made, 1)

            def make_silu(i, t):
                act.wait_ge(gate_done, BT * i + t + 1)
                wait(act, hidden_made, BT * i + t - 1)
                nc.scalar.activation(silu[:, t % 2], gate_ps[:, t % 2], ACT.Silu).then_inc(silu_made, 1)

            def keep_hidden(i, t):
                act.wait_ge(hidden_turned, BT * i + t + 1)
                wait(act, down_done, BT * i + t - 1)
                nc.scalar.copy(hidden_t[:, t % 2], hidden_ps[:]).then_inc(hidden_t_kept, 1)

            def block_step(i, odd, nxt):
                def front(part):
                    if nxt is not None:
                        part(i + 1, nxt, 1 - odd)

                make_silu(i, 0)
                front(keep_heads)
                make_silu(i, 1)
                keep_hidden(i, 0)
                make_silu(i, 2)
                keep_hidden(i, 1)
                make_silu(i, 3)
                keep_hidden(i, 2)
                front(keep_xf)
                keep_hidden(i, 3)
                front(scale_rows)

            def step(batch):
                block_step(2 * batch, 0, batch)
                last = isinstance(batch, int) and batch == BATCH - 1
                block_step(2 * batch + 1, 1, None if last else batch + 1)

            keep_heads(0, 0, 0)
            keep_xf(0, 0, 0)
            scale_rows(0, 0, 0)
            by_batch(act, step)

        @block.vector
        def _(dve):
            state = {"n": 0}

            def link(i, instruction):
                state["n"] += 1
                instruction.then_inc(front_step, 1)
                dve.wait_ge(front_step, VEC_STEPS * i + state["n"])

            def take_moments(i, source):
                for t in range(BT):
                    last = nc.vector.bn_stats(stats[:, t], source[:, t])
                link(i, last)
                stand(dve, dve_stood)
                for t in range(BT):
                    last = nc.vector.bn_aggr(moments[:, t], stats[:, t])
                last.then_inc(moments_made, 1)

            def add_heads(i, batch, odd):
                state["n"] = 0
                dve.wait_ge(wo_done, i + 1)
                dve.wait_ge(res_in[odd], 16 * (batch + 1))
                link(i, nc.vector.tensor_tensor(
                    res[:, odd].rearrange("p t d -> p (t d)"), front_ps[:].rearrange("p c n -> p (c n)"),
                    res[:, odd].rearrange("p t d -> p (t d)"), ALU.add))
                wait(dve, rstd_made, 2 * i)
                take_moments(i, res[:, odd])

            def norm_first(i, batch, odd):
                dve.wait_ge(rstd_made, 2 * i + 1)
                wait(dve, added, BT * (i - 1))
                for t in range(BT):
                    last = nc.vector.tensor_scalar(x1[:, odd, t], res[:, odd, t], moments[:, t, 0:1],
                                                   rstd[:, t:t + 1], ALU.subtract, ALU.mult)
                link(i, last)
                take_moments(i, x1[:, odd])

            def norm_second(i, batch, odd):
                dve.wait_ge(rstd_made, 2 * i + 2)
                wait(dve, row_made, i)
                for t in range(BT):
                    last = nc.vector.scalar_tensor_tensor(xf[:, t], x1[:, odd, t], moments[:, t, 0:1], ln_w[:],
                                                          ALU.subtract, ALU.mult)
                link(i, last)
                for t in range(BT):
                    last = nc.vector.scalar_tensor_tensor(xf[:, t], xf[:, t], rstd[:, t:t + 1], ln_b[:],
                                                          ALU.mult, ALU.add)
                last.then_inc(xf_made, 1)

            def choose(i, batch, odd):
                dve.wait_ge(routed, i + 1)
                wait(dve, tanh_made, i)
                logits = front_ps[:, 0, :BT * EXPERTS].rearrange("p (t e) -> p t e", e=EXPERTS)
                wide = [P, BT, EXPERTS]
                nc.vector.tensor_reduce(top[:], logits, X, ALU.max).then_inc(top_made, 1)
                dve.wait_ge(top_made, i + 1)
                link(i, nc.vector.tensor_tensor(is_top[:], logits, top[:].unsqueeze(2).to_broadcast(wide), ALU.is_ge))
                link(i, nc.vector.scalar_tensor_tensor(candidate[:], is_top[:], -float(EXPERTS), number[:],
                                                       ALU.mult, ALU.add))
                link(i, nc.vector.tensor_reduce(first[:], candidate[:], X, ALU.min))
                link(i, nc.vector.tensor_scalar(first[:], first[:], float(EXPERTS), None, ALU.add))
                link(i, nc.vector.tensor_tensor(chosen[:], number[:], first[:].unsqueeze(2).to_broadcast(wide),
                                                ALU.is_equal))
                wait(dve, ranked, i)
                nc.vector.tensor_copy(chosen_bf[:, :BT], chosen[:]).then_inc(chosen_made, 1)
                link(i, nc.vector.tensor_copy(chosen_all[:, bass.ds(BT * i, BT)], chosen[:]))
                dve.wait_ge(tanh_made, i + 1)
                wait(dve, row_made, i)
                nc.vector.tensor_scalar(score[:, 1], score[:, 0], 0.5, 0.5, ALU.mult, ALU.add).then_inc(score_made, 1)

            def find_place(i, batch, odd):
                dve.wait_ge(ranked, i + 1)
                wide = [P, BT, EXPERTS]
                ranks = front_ps[:, 1, :(BT + 1) * EXPERTS].rearrange("p (t e) -> p t e", e=EXPERTS)
                link(i, nc.vector.tensor_tensor(rank[:], ranks[:, :BT],
                                                counts[:].unsqueeze(1).to_broadcast(wide), ALU.add))
                link(i, nc.vector.tensor_tensor(counts[:], counts[:], ranks[:, BT], ALU.add))
                link(i, nc.vector.tensor_tensor(rank[:], rank[:], chosen[:], ALU.mult))
                link(i, nc.vector.tensor_reduce(rank_all[:, bass.ds(BT * i, BT)], rank[:], X, ALU.add))
                link(i, nc.vector.scalar_tensor_tensor(place[:], first[:], float(REGION),
                                                       rank_all[:, bass.ds(BT * i, BT)], ALU.mult, ALU.add))
                wait(dve, scattered, 16 * BT * (i - 1))
                nc.vector.tensor_copy(place_i[:, odd], place[:]).then_inc(placed, 1)
                while state["n"] < VEC_STEPS:
                    link(i, nc.vector.tensor_copy(place[:, :1], place[:, 1:2]))

            def times_up(i, t):
                dve.wait_ge(silu_made, BT * i + t + 1)
                dve.wait_ge(up_done, BT * i + t + 1)
                wait(dve, hidden_turned, BT * i + t - 1)
                nc.vector.tensor_tensor(hidden[:, t % 2], silu[:, t % 2], up_ps[:, t % 2],
                                        ALU.mult).then_inc(hidden_made, 1)

            def add_shared(i, t, odd):
                dve.wait_ge(down_done, BT * i + t + 1)
                nc.vector.scalar_tensor_tensor(acc[:, BT * i + t], x1[:, odd, t], 2.0, down_ps[:],
                                               ALU.mult, ALU.add).then_inc(added, 1)

            def block_step(i, odd, nxt):
                def front(part):
                    if nxt is not None:
                        part(i + 1, nxt, 1 - odd)

                times_up(i, 0)
                times_up(i, 1)
                front(add_heads)
                add_shared(i, 0, odd)
                front(norm_first)
                times_up(i, 2)
                add_shared(i, 1, odd)
                front(norm_second)
                times_up(i, 3)
                add_shared(i, 2, odd)
                front(choose)
                add_shared(i, 3, odd)
                front(find_place)

            def step(batch):
                block_step(2 * batch, 0, batch)
                last = isinstance(batch, int) and batch == BATCH - 1
                block_step(2 * batch + 1, 1, None if last else batch + 1)

            nc.vector.memset(counts[:], 0.0).then_inc(vec_const, 1)
            nc.vector.memset(chosen_bf[:], 0.0).then_inc(vec_const, 1)
            dve.wait_ge(vec_const, 2)
            dve.wait_ge(const_step, 6)
            dve.wait_ge(small_in, 16 * 3)
            for part in (add_heads, norm_first, norm_second, choose, find_place):
                part(0, 0, 0)
            by_batch(dve, step)

        @block.gpsimd
        def _(pool):
            nc.gpsimd.memset(minus_half[:], -0.5).then_inc(const_step, 1)
            nc.gpsimd.memset(ones[:], 1.0).then_inc(const_step, 1)
            nc.gpsimd.memset(before[:], 1.0).then_inc(const_step, 1)
            nc.gpsimd.iota(number_i[:], pattern=[[0, BT], [1, EXPERTS]], base=0,
                           channel_multiplier=0).then_inc(const_step, 1)
            pool.wait_ge(const_step, 4)
            nc.gpsimd.tensor_copy(number[:], number_i[:]).then_inc(const_step, 1)
            nc.gpsimd.affine_select(out=before[:], in_=before[:], compare_op=ALU.is_gt, fill=0.0, base=0,
                                    pattern=[[1, P]], channel_multiplier=-1).then_inc(const_step, 1)
            pool.wait_ge(const_step, 6)

            def make_rstd(i, which):
                k = 2 * i + which
                pool.wait_ge(moments_made, k + 1)
                stand(pool, pool_stood)
                nc.gpsimd.tensor_scalar(var_eps[:], moments[:, :, 1], EPS, None, ALU.add).then_inc(pool_step, 1)
                pool.wait_ge(pool_step, k + 1)
                nc.gpsimd.tensor_tensor(rstd[:], var_eps[:], minus_half[:], ALU.pow).then_inc(rstd_made, 1)

            def scatter(i, odd):
                pool.wait_ge(placed, i + 1)
                pool.wait_ge(row_made, i + 1)
                stand(pool, pool_stood)
                for t in range(BT):
                    nc.gpsimd.indirect_dma_start(
                        scratch["rows"], bass.IndirectOffsetOnAxis(place_i[:, odd, t:t + 1], 0),
                        row[:, t], None).then_inc(scattered, 16)

            def front(i, odd):
                make_rstd(i, 0)
                make_rstd(i, 1)
                scatter(i, odd)

            def step(batch):
                front(2 * batch + 1, 1)
                if not (isinstance(batch, int) and batch == BATCH - 1):
                    front(2 * batch + 2, 0)

            front(0, 0)
            by_batch(pool, step)
            pool.wait_ge(scattered, 16 * BT * BLOCKS)


def experts(nc, io, keep, scratch, out):
    ident, acc, gate_w, up_w, down_w = keep["ident"], keep["acc"], keep["gate"], keep["up"], keep["down"]
    chosen_all, rank_all, counts = keep["chosen_all"], keep["rank_all"], keep["counts"]
    with ExitStack() as ctx:
        b = Bufs(nc, ctx)
        zeros = b.sb("zeros", [P, D])
        lane_i = b.sb("lane_i", [P, EXPERTS], I32)
        tail = b.sb("tail", [P, EXPERTS])
        tail_i = b.sb("tail_i", [P, EXPERTS], I32)
        ceil_i = b.sb("ceil_i", [P, EXPERTS], I32)
        tiles = b.sb("tiles", [P, EXPERTS])
        ones_e = b.sb("ones_e", [P, EXPERTS])
        ends = b.sb("ends", [P, EXPERTS])
        starts = b.sb("starts", [P, EXPERTS])
        start_rows = b.sb("start_rows", [P, EXPERTS])
        slot_i = b.sb("slot_i", [P, SLOTS], I32)
        slot = b.sb("slot", [P, SLOTS])
        begun = b.sb("begun", [P, SLOTS, EXPERTS])
        owner = b.sb("owner", [P, SLOTS])
        base = b.sb("base", [P, SLOTS])
        owner_i = b.sb("owner_i", [P, SLOTS], I32)
        source_i = b.sb("source_i", [P, SLOTS], I32)
        fetch = b.sb("fetch", [P, TILES])
        fetch_wide = b.sb("fetch_wide", [P, TILES, EXPERTS])
        fetch_i = b.sb("fetch_i", [P, 2, BT], I32)
        rows = b.sb("rows_in", [P, 2, D])
        rows_t = b.sb("rows_t", [P, 2, D])
        silu = b.sb("silu_e", [P, 2, INNER])
        hidden = b.sb("hidden_e", [P, 2, INNER])
        hidden_t = b.sb("hidden_t_e", [P, 2, INNER])
        result = b.sb("result", [P, 2, D])
        fetched = b.sb("fetched", [P, 2, BT, D])
        stats = b.sb("stats_e", [P, BT, 6])
        moments = b.sb("moments_e", [P, BT, 2])
        var_eps = b.sb("var_eps_e", [P, BT])
        rstd = b.sb("rstd_e", [P, BT])
        minus_half = b.sb("minus_half_e", [P, BT])
        final = b.sb("final", [P, 2, BT, D])
        gate_ps = b.ps("gate_ps_e", [P, 2, INNER])
        up_ps = b.ps("up_ps_e", [P, 2, INNER])
        hidden_ps = b.ps("hidden_ps_e", [P, INNER])
        down_ps = b.ps("down_ps_e", [P, D])
        rows_ps = b.ps("rows_ps", [P, D])

        pool_const, tails_set, table_step, tables_made = (
            b.sem("pool_const_e"), b.sem("tails_set"), b.sem("table_step"), b.sem("tables_made"))
        tail_made = b.sem("tail_made")
        rows_in = [b.sem(f"rows_in{r}") for r in range(2)]
        rows_turned, rows_t_kept = b.sem("rows_turned"), b.sem("rows_t_kept")
        gate_done, up_done, silu_made, hidden_made = (
            b.sem("gate_done_e"), b.sem("up_done_e"), b.sem("silu_made_e"), b.sem("hidden_made_e"))
        hidden_turned, hidden_t_kept, down_done, result_made = (
            b.sem("hidden_turned_e"), b.sem("hidden_t_kept_e"), b.sem("down_done_e"), b.sem("result_made"))
        result_stored = [b.sem("result_stored0"), b.sem("result_stored1")]
        fetch_made, fetched_in = b.sem("fetch_made"), [b.sem("fetched_in0"), b.sem("fetched_in1")]
        summed, moments_made, pool_step, rstd_made, final_made = (
            b.sem("summed"), b.sem("moments_made_e"), b.sem("pool_step_e"), b.sem("rstd_made_e"), b.sem("final_made"))
        stats_made = b.sem("stats_made")
        out_stored = [b.sem("out_stored0"), b.sem("out_stored1")]
        dve_stood, pool_stood = b.sem("dve_stood"), b.sem("pool_stood")
        block = ctx.enter_context(nc.Block())
        out_blocks = out.rearrange("(n t p) d -> n p t d", t=BT, p=P)

        def by_pair(eng, step):
            step(0)
            with eng.Fori(1, SLOTS // 2 - 1) as pair:
                step(pair)
            step(SLOTS // 2 - 1)

        def inside(j):
            return not isinstance(j, int) or j < SLOTS

        @block.sync
        def _(sp):
            def load(j, odd, pair):
                if inside(j):
                    wait(sp, rows_turned, j - 1)
                    start = sp.value_load(source_i[0:1, bass.ds(j, 1)], min_val=0,
                                          max_val=EXPERTS * REGION - P)
                    sp.dma_start(rows[:, odd], scratch["rows"][bass.ds(start, P)]).then_inc(rows_in[odd], 16)

            def store(j, odd):
                sp.wait_ge(result_made, j + 1)
                sp.dma_start(scratch["results"][bass.ds(j * P, P)], result[:, odd]).then_inc(result_stored[odd], 16)

            sp.wait_ge(tails_set, 16 * EXPERTS)
            sp.wait_ge(tables_made, 1)
            load(0, 0, 0)
            load(1, 1, 0)

            def step(pair):
                load(2 * pair + 2, 0, pair + 1)
                store(2 * pair, 0)
                load(2 * pair + 3, 1, pair + 1)
                store(2 * pair + 1, 1)

            by_pair(sp, step)

            def store_out(batch):
                for odd in range(2):
                    i = 2 * batch + odd
                    sp.wait_ge(final_made, i + 1)
                    sp.dma_start(out_blocks[i], final[:, odd]).then_inc(out_stored[odd], 16)

            by_batch(sp, store_out)
            for odd in range(2):
                sp.wait_ge(out_stored[odd], 16 * BATCH)

        @block.tensor
        def _(pe):
            def turn_rows(j, odd, pair):
                if not inside(j):
                    return
                pe.wait_ge(rows_in[odd], 16 * (pair + 1))
                wait(pe, rows_t_kept, j)
                for c in range(DC):
                    last = nc.tensor.transpose(rows_ps[:, c * P:(c + 1) * P], rows[:, odd, c * P:(c + 1) * P],
                                               ident[:])
                last.then_inc(rows_turned, 1)

            def product(j, odd, weights, bank, used, done):
                if not inside(j):
                    return
                e = pe.value_load(owner_i[0:1, bass.ds(j, 1)], min_val=0, max_val=EXPERTS - 1)
                pe.wait_ge(rows_t_kept, j + 1)
                wait(pe, used, j - 1)
                for c in range(DC):
                    last = nc.tensor.matmul(bank[:, odd], rows_t[:, odd, c * P:(c + 1) * P], weights[:, e, c],
                                            start=(c == 0), stop=(c == DC - 1))
                last.then_inc(done, 1)

            def turn_hidden(j, odd):
                pe.wait_ge(hidden_made, j + 1)
                wait(pe, hidden_t_kept, j)
                for c in range(IC):
                    last = nc.tensor.transpose(hidden_ps[:, c * P:(c + 1) * P],
                                               hidden[:, odd, c * P:(c + 1) * P], ident[:])
                last.then_inc(hidden_turned, 1)

            def down(j, odd):
                e = pe.value_load(owner_i[0:1, bass.ds(j, 1)], min_val=0, max_val=EXPERTS - 1)
                pe.wait_ge(hidden_t_kept, j + 1)
                wait(pe, result_made, j)
                for c in range(IC):
                    last = nc.tensor.matmul(down_ps[:], hidden_t[:, odd, c * P:(c + 1) * P], down_w[:, e, c],
                                            start=(c == 0), stop=(c == IC - 1))
                last.then_inc(down_done, 1)

            def step(pair):
                for odd in range(2):
                    j = 2 * pair + odd
                    product(j + 1, 1 - odd, gate_w, gate_ps, silu_made, gate_done)
                    turn_hidden(j, odd)
                    product(j + 1, 1 - odd, up_w, up_ps, hidden_made, up_done)
                    down(j, odd)
                    turn_rows(j + 2, odd, pair + 1)

            pe.wait_ge(tables_made, 1)
            pe.wait_ge(keep["weights_in"], 16 * 2 * EXPERTS)
            pe.wait_ge(keep["down_in"], 16 * EXPERTS)
            turn_rows(0, 0, 0)
            turn_rows(1, 1, 0)
            product(0, 0, gate_w, gate_ps, silu_made, gate_done)
            product(0, 0, up_w, up_ps, hidden_made, up_done)
            by_pair(pe, step)

        @block.scalar
        def _(act):
            def keep_rows(j, odd):
                if inside(j):
                    act.wait_ge(rows_turned, j + 1)
                    wait(act, up_done, j - 1)
                    nc.scalar.copy(rows_t[:, odd], rows_ps[:]).then_inc(rows_t_kept, 1)

            def make_silu(j, odd):
                if inside(j):
                    act.wait_ge(gate_done, j + 1)
                    wait(act, hidden_made, j - 1)
                    nc.scalar.activation(silu[:, odd], gate_ps[:, odd], ACT.Silu).then_inc(silu_made, 1)

            def keep_hidden(j, odd):
                act.wait_ge(hidden_turned, j + 1)
                wait(act, down_done, j - 1)
                nc.scalar.copy(hidden_t[:, odd], hidden_ps[:]).then_inc(hidden_t_kept, 1)

            def step(pair):
                for odd in range(2):
                    j = 2 * pair + odd
                    make_silu(j + 1, 1 - odd)
                    keep_hidden(j, odd)
                    keep_rows(j + 2, odd)

            keep_rows(0, 0)
            keep_rows(1, 1)
            make_silu(0, 0)
            by_pair(act, step)

        @block.vector
        def _(dve):
            count = [0]

            def link(instruction):
                count[0] += 1
                instruction.then_inc(table_step, 1)
                dve.wait_ge(table_step, count[0])

            dve.wait_ge(pool_const, 4)
            link(nc.vector.tensor_copy(tail[:], lane_i[:]))
            link(nc.vector.tensor_tensor(tail[:], tail[:], counts[:], ALU.add))
            nc.vector.tensor_copy(tail_i[:], tail[:]).then_inc(tail_made, 1)
            link(nc.vector.tensor_scalar(tiles[:], counts[:], float(P - 1), None, ALU.add))
            link(nc.vector.tensor_copy(ceil_i[:], tiles[:]))
            link(nc.vector.tensor_scalar(ceil_i[:], ceil_i[:], P.bit_length() - 1, None, ALU.arith_shift_right))
            link(nc.vector.tensor_copy(tiles[:], ceil_i[:]))
            link(nc.vector.tensor_tensor_scan(ends[:], ones_e[:], tiles[:], 0.0, ALU.mult, ALU.add))
            link(nc.vector.tensor_tensor(starts[:], ends[:], tiles[:], ALU.subtract))
            link(nc.vector.tensor_copy(slot[:], slot_i[:]))
            link(nc.vector.tensor_scalar(base[:, 0:1], ends[:, EXPERTS - 1:], -1.0, None, ALU.add))
            link(nc.vector.tensor_scalar(slot[:], slot[:], base[:, 0:1], None, ALU.min))
            wide = [P, SLOTS, EXPERTS]
            starts_wide = starts[:].unsqueeze(1).to_broadcast(wide)
            link(nc.vector.tensor_tensor(begun[:], starts_wide, slot[:].unsqueeze(2).to_broadcast(wide), ALU.is_le))
            link(nc.vector.tensor_reduce(owner[:], begun[:], X, ALU.add))
            link(nc.vector.tensor_scalar(owner[:], owner[:], -1.0, None, ALU.add))
            link(nc.vector.tensor_copy(owner_i[:], owner[:]))
            link(nc.vector.tensor_tensor(begun[:], begun[:], starts_wide, ALU.mult))
            link(nc.vector.tensor_reduce(base[:], begun[:], X, ALU.max))
            link(nc.vector.tensor_tensor(base[:], slot[:], base[:], ALU.subtract))
            link(nc.vector.tensor_scalar(base[:], base[:], float(P), None, ALU.mult))
            link(nc.vector.scalar_tensor_tensor(base[:], owner[:], float(REGION), base[:], ALU.mult, ALU.add))
            nc.vector.tensor_copy(source_i[:], base[:]).then_inc(tables_made, 1)
            wide = [P, TILES, EXPERTS]
            link(nc.vector.tensor_scalar(start_rows[:], starts[:], float(P), None, ALU.mult))
            link(nc.vector.tensor_tensor(fetch_wide[:], chosen_all[:], start_rows[:].unsqueeze(1).to_broadcast(wide),
                                         ALU.mult))
            link(nc.vector.tensor_reduce(fetch[:], fetch_wide[:], X, ALU.add))
            link(nc.vector.tensor_tensor(fetch[:], fetch[:], rank_all[:], ALU.add))

            def times_up(j, odd):
                if inside(j):
                    dve.wait_ge(silu_made, j + 1)
                    dve.wait_ge(up_done, j + 1)
                    wait(dve, hidden_turned, j - 1)
                    nc.vector.tensor_tensor(hidden[:, odd], silu[:, odd], up_ps[:, odd],
                                            ALU.mult).then_inc(hidden_made, 1)

            def keep_result(j, odd, pair):
                dve.wait_ge(down_done, j + 1)
                wait(dve, result_stored[odd], 16 * pair)
                nc.vector.tensor_copy(result[:, odd], down_ps[:]).then_inc(result_made, 1)

            def step(pair):
                for odd in range(2):
                    j = 2 * pair + odd
                    times_up(j + 1, 1 - odd)
                    keep_result(j, odd, pair)

            times_up(0, 0)
            by_pair(dve, step)

            def finish(batch):
                for odd in range(2):
                    i = 2 * batch + odd
                    if not (isinstance(batch, int) and batch == BATCH - 1 and odd):
                        wait(dve, fetched_in[1 - odd], 16 * BT * (batch + odd))
                        nc.vector.tensor_copy(fetch_i[:, 1 - odd],
                                              fetch[:, bass.ds(BT * i + BT, BT)]).then_inc(fetch_made, 1)
                    dve.wait_ge(fetched_in[odd], 16 * BT * (batch + 1))
                    flat = "p t d -> p (t d)"
                    nc.vector.tensor_tensor(fetched[:, odd].rearrange(flat), fetched[:, odd].rearrange(flat),
                                            acc[:, bass.ds(BT * i, BT)].rearrange(flat), ALU.add).then_inc(summed, 1)
                    dve.wait_ge(summed, i + 1)
                    for t in range(BT):
                        last = nc.vector.bn_stats(stats[:, t], fetched[:, odd, t])
                    last.then_inc(stats_made, 1)
                    dve.wait_ge(stats_made, i + 1)
                    stand(dve, dve_stood)
                    for t in range(BT):
                        last = nc.vector.bn_aggr(moments[:, t], stats[:, t])
                    last.then_inc(moments_made, 1)
                    dve.wait_ge(rstd_made, i + 1)
                    wait(dve, out_stored[odd], 16 * batch)
                    for t in range(BT):
                        last = nc.vector.tensor_scalar(final[:, odd, t], fetched[:, odd, t], moments[:, t, 0:1],
                                                       rstd[:, t:t + 1], ALU.subtract, ALU.mult)
                    last.then_inc(final_made, 1)

            nc.vector.tensor_copy(fetch_i[:, 0], fetch[:, 0:BT]).then_inc(fetch_made, 1)
            by_batch(dve, finish)

        @block.gpsimd
        def _(pool):
            nc.gpsimd.memset(zeros[:], 0.0).then_inc(pool_const, 1)
            nc.gpsimd.memset(ones_e[:], 1.0).then_inc(pool_const, 1)
            nc.gpsimd.iota(lane_i[:], pattern=[[REGION, EXPERTS]], base=0, channel_multiplier=1).then_inc(pool_const, 1)
            nc.gpsimd.iota(slot_i[:], pattern=[[1, SLOTS]], base=0, channel_multiplier=0).then_inc(pool_const, 1)
            nc.gpsimd.memset(minus_half[:], -0.5).then_inc(pool_const, 1)
            pool.wait_ge(pool_const, 5)
            pool.wait_ge(tail_made, 1)
            for e in range(EXPERTS):
                nc.gpsimd.indirect_dma_start(scratch["rows"], bass.IndirectOffsetOnAxis(tail_i[:, e:e + 1], 0),
                                             zeros[:], None).then_inc(tails_set, 16)
            for odd in range(2):
                pool.wait_ge(result_stored[odd], 16 * (SLOTS // 2))

            def fetch_block(i, odd):
                pool.wait_ge(fetch_made, i + 1)
                wait(pool, final_made, i - 1)
                stand(pool, pool_stood)
                for t in range(BT):
                    nc.gpsimd.indirect_dma_start(
                        fetched[:, odd, t], None, scratch["results"],
                        bass.IndirectOffsetOnAxis(fetch_i[:, odd, t:t + 1], 0)).then_inc(fetched_in[odd], 16)

            def make_rstd(i):
                pool.wait_ge(moments_made, i + 1)
                stand(pool, pool_stood)
                nc.gpsimd.tensor_scalar(var_eps[:], moments[:, :, 1], EPS, None, ALU.add).then_inc(pool_step, 1)
                pool.wait_ge(pool_step, i + 1)
                nc.gpsimd.tensor_tensor(rstd[:], var_eps[:], minus_half[:], ALU.pow).then_inc(rstd_made, 1)

            fetch_block(0, 0)

            def step(batch):
                fetch_block(2 * batch + 1, 1)
                make_rstd(2 * batch)
                if not (isinstance(batch, int) and batch == BATCH - 1):
                    fetch_block(2 * batch + 2, 0)
                make_rstd(2 * batch + 1)

            by_batch(pool, step)


def layer(nc, io, out):
    scratch = {
        "qk": [nc.dram_tensor(f"{n}_parts", [UNITS, PARTS, GD, SEQ], BF16).ap() for n in "qk"],
        "heads": nc.dram_tensor("heads_rows", [UNITS, 2, P, BT * GD], F32).ap(),
        "rows": nc.dram_tensor("expert_rows", [EXPERTS * REGION, D], F32).ap(),
        "results": nc.dram_tensor("expert_results", [SLOTS * P, D], F32).ap(),
    }
    with ExitStack() as ctx:
        b = Bufs(nc, ctx)
        keep = {
            "ident": b.sb("ident", [P, P]),
            "wo_t": b.sb("wo_t", [P, DC, D]),
            "gate": b.sb("gate_sb", [P, EXPERTS, DC, INNER]),
            "up": b.sb("up_sb", [P, EXPERTS, DC, INNER]),
            "weights_in": b.sem("weights_in"),
            "down_in": b.sem("down_in"),
        }
        shared = b.sb("v_then_sum", [P, TOKENS * D // P])
        keep["v_all"] = shared[:].rearrange("p (u t e) -> p u t e", u=UNITS, t=SEQ_TILES)
        keep["acc"] = shared[:].rearrange("p (t d) -> p t d", d=D)
        project(nc, io, keep, scratch)
        attend(nc, io, keep, scratch)
        keep["down"] = b.sb("down_sb", [P, EXPERTS, IC, D])
        keep["chosen_all"] = b.sb("chosen_all", [P, TILES, EXPERTS])
        keep["rank_all"] = b.sb("rank_all", [P, TILES])
        keep["counts"] = b.sb("counts", [P, EXPERTS])
        mix(nc, io, keep, scratch)
        experts(nc, io, keep, scratch, out)


_INPUTS = {
    "x": "L0_attn_x", "Wq": "L0_attn_Wq", "Wk": "L0_attn_Wk", "Wv": "L0_attn_Wv", "Wo": "L0_attn_Wo",
    "ln_w": "L0_ffn_ln_w", "ln_b": "L0_ffn_ln_b", "router_w": "L0_ffn_router_w", "gate_w": "L0_ffn_gate_w",
    "up_w": "L0_ffn_up_w", "down_w": "L0_ffn_down_w", "sh_gate": "L0_ffn_sh_gate", "sh_up": "L0_ffn_sh_up",
    "sh_down": "L0_ffn_sh_down",
}


def kernel(**inputs):
    from concourse import bacc
    from concourse.bass_utils import run_bass_kernel_spmd

    arrays = {name: np.ascontiguousarray(inputs[given]) for name, given in _INPUTS.items()}
    shape = arrays["x"].shape
    arrays["x"] = arrays["x"].reshape(TOKENS, D)
    arrays["cos"], arrays["sin"] = rope_tables()
    nc = bacc.Bacc("TRN2", target_bir_lowering=False, num_devices=1)
    io = {name: nc.dram_tensor(f"in_{name}", a.shape, mybir.dt.from_np(a.dtype), kind="ExternalInput").ap()
          for name, a in arrays.items()}
    out = nc.dram_tensor("out", [TOKENS, D], F32, kind="ExternalOutput").ap()
    layer(nc, io, out)
    result = run_bass_kernel_spmd(nc, [{f"in_{name}": a for name, a in arrays.items()}], core_ids=[0])
    return result.results[0]["out"].reshape(shape)
```
